# Optimizing a Trainium2 kernel written in Bass

```python
import numpy as np
import jax
import jax.numpy as jnp

def _softmax(x, axis=-1):
    return jax.nn.softmax(x, axis=axis)

def _gelu(x):
    return jax.nn.gelu(x, approximate=True)

def _silu(x):
    return jax.nn.silu(x)

def _sigmoid(x):
    return jax.nn.sigmoid(x)

def _layernorm(x, axis=-1, eps=1e-05):
    m = jnp.mean(x, axis=axis, keepdims=True)
    v = jnp.var(x, axis=axis, keepdims=True)
    return (x - m) / jnp.sqrt(v + eps)

def _scatter_add(tgt, idx, src, axis=0):
    return tgt.at[idx].add(src)

def _segment_sum(src, seg, n):
    return jax.ops.segment_sum(src, seg, n)
kernel_name = 'mk_dlrm_tower_d1_rec_r8_426d9d'

def setup_inputs(seed: int=0):
    np.random.seed(seed)
    _w = jnp.asarray

    def _rec_inputs():
        import jax
        import jax.numpy as jnp
        _tk = jax.random.key(seed)
        dense_ctx = jax.random.normal(jax.random.fold_in(_tk, 190), (512, 16), jnp.float32)
        ids = jnp.stack([jax.random.randint(jax.random.fold_in(_tk, 200 + f), (512,), 0, v, jnp.int32) for f, v in enumerate([125000, 1250, 125000, 1250, 12500, 1000, 1000, 1000, 125000, 1250, 12500, 12500, 1250, 1250, 1000, 12500, 1250, 12500, 1000, 1000, 1250, 1000, 1250, 1250, 1250, 1250, 12500, 1000, 12500, 1250, 1250, 1000, 1000, 1250, 1250, 1250, 1000, 1250, 1000])], axis=1)
        tbl_0 = 0.05 * jax.random.normal(jax.random.fold_in(_tk, 500 + 0), (125000, 64), jnp.float32)
        tbl_1 = 0.05 * jax.random.normal(jax.random.fold_in(_tk, 500 + 1), (1250, 64), jnp.float32)
        tbl_2 = 0.05 * jax.random.normal(jax.random.fold_in(_tk, 500 + 2), (125000, 64), jnp.float32)
        tbl_3 = 0.05 * jax.random.normal(jax.random.fold_in(_tk, 500 + 3), (1250, 64), jnp.float32)
        tbl_4 = 0.05 * jax.random.normal(jax.random.fold_in(_tk, 500 + 4), (12500, 64), jnp.float32)
        tbl_5 = 0.05 * jax.random.normal(jax.random.fold_in(_tk, 500 + 5), (1000, 64), jnp.float32)
        tbl_6 = 0.05 * jax.random.normal(jax.random.fold_in(_tk, 500 + 6), (1000, 64), jnp.float32)
        tbl_7 = 0.05 * jax.random.normal(jax.random.fold_in(_tk, 500 + 7), (1000, 64), jnp.float32)
        tbl_8 = 0.05 * jax.random.normal(jax.random.fold_in(_tk, 500 + 8), (125000, 64), jnp.float32)
        tbl_9 = 0.05 * jax.random.normal(jax.random.fold_in(_tk, 500 + 9), (1250, 64), jnp.float32)
        tbl_10 = 0.05 * jax.random.normal(jax.random.fold_in(_tk, 500 + 10), (12500, 64), jnp.float32)
        tbl_11 = 0.05 * jax.random.normal(jax.random.fold_in(_tk, 500 + 11), (12500, 64), jnp.float32)
        tbl_12 = 0.05 * jax.random.normal(jax.random.fold_in(_tk, 500 + 12), (1250, 64), jnp.float32)
        tbl_13 = 0.05 * jax.random.normal(jax.random.fold_in(_tk, 500 + 13), (1250, 64), jnp.float32)
        tbl_14 = 0.05 * jax.random.normal(jax.random.fold_in(_tk, 500 + 14), (1000, 64), jnp.float32)
        tbl_15 = 0.05 * jax.random.normal(jax.random.fold_in(_tk, 500 + 15), (12500, 64), jnp.float32)
        tbl_16 = 0.05 * jax.random.normal(jax.random.fold_in(_tk, 500 + 16), (1250, 64), jnp.float32)
        tbl_17 = 0.05 * jax.random.normal(jax.random.fold_in(_tk, 500 + 17), (12500, 64), jnp.float32)
        tbl_18 = 0.05 * jax.random.normal(jax.random.fold_in(_tk, 500 + 18), (1000, 64), jnp.float32)
        tbl_19 = 0.05 * jax.random.normal(jax.random.fold_in(_tk, 500 + 19), (1000, 64), jnp.float32)
        tbl_20 = 0.05 * jax.random.normal(jax.random.fold_in(_tk, 500 + 20), (1250, 64), jnp.float32)
        tbl_21 = 0.05 * jax.random.normal(jax.random.fold_in(_tk, 500 + 21), (1000, 64), jnp.float32)
        tbl_22 = 0.05 * jax.random.normal(jax.random.fold_in(_tk, 500 + 22), (1250, 64), jnp.float32)
        tbl_23 = 0.05 * jax.random.normal(jax.random.fold_in(_tk, 500 + 23), (1250, 64), jnp.float32)
        tbl_24 = 0.05 * jax.random.normal(jax.random.fold_in(_tk, 500 + 24), (1250, 64), jnp.float32)
        tbl_25 = 0.05 * jax.random.normal(jax.random.fold_in(_tk, 500 + 25), (1250, 64), jnp.float32)
        tbl_26 = 0.05 * jax.random.normal(jax.random.fold_in(_tk, 500 + 26), (12500, 64), jnp.float32)
        tbl_27 = 0.05 * jax.random.normal(jax.random.fold_in(_tk, 500 + 27), (1000, 64), jnp.float32)
        tbl_28 = 0.05 * jax.random.normal(jax.random.fold_in(_tk, 500 + 28), (12500, 64), jnp.float32)
        tbl_29 = 0.05 * jax.random.normal(jax.random.fold_in(_tk, 500 + 29), (1250, 64), jnp.float32)
        tbl_30 = 0.05 * jax.random.normal(jax.random.fold_in(_tk, 500 + 30), (1250, 64), jnp.float32)
        tbl_31 = 0.05 * jax.random.normal(jax.random.fold_in(_tk, 500 + 31), (1000, 64), jnp.float32)
        tbl_32 = 0.05 * jax.random.normal(jax.random.fold_in(_tk, 500 + 32), (1000, 64), jnp.float32)
        tbl_33 = 0.05 * jax.random.normal(jax.random.fold_in(_tk, 500 + 33), (1250, 64), jnp.float32)
        tbl_34 = 0.05 * jax.random.normal(jax.random.fold_in(_tk, 500 + 34), (1250, 64), jnp.float32)
        tbl_35 = 0.05 * jax.random.normal(jax.random.fold_in(_tk, 500 + 35), (1250, 64), jnp.float32)
        tbl_36 = 0.05 * jax.random.normal(jax.random.fold_in(_tk, 500 + 36), (1000, 64), jnp.float32)
        tbl_37 = 0.05 * jax.random.normal(jax.random.fold_in(_tk, 500 + 37), (1250, 64), jnp.float32)
        tbl_38 = 0.05 * jax.random.normal(jax.random.fold_in(_tk, 500 + 38), (1000, 64), jnp.float32)
        _rk = jax.random.fold_in(_tk, 7)
        W_top1 = 0.0363456 * jax.random.normal(jax.random.fold_in(_tk, 801), (757, 512), jnp.float32)
        W_top2 = 0.0441942 * jax.random.normal(jax.random.fold_in(_tk, 802), (512, 256), jnp.float32)
        W_top3 = 0.0625 * jax.random.normal(jax.random.fold_in(_tk, 803), (256, 1), jnp.float32)
        b_top1 = jnp.zeros((512,), jnp.float32)
        b_top2 = jnp.zeros((256,), jnp.float32)
        return (dense_ctx, ids, tbl_0, tbl_1, tbl_2, tbl_3, tbl_4, tbl_5, tbl_6, tbl_7, tbl_8, tbl_9, tbl_10, tbl_11, tbl_12, tbl_13, tbl_14, tbl_15, tbl_16, tbl_17, tbl_18, tbl_19, tbl_20, tbl_21, tbl_22, tbl_23, tbl_24, tbl_25, tbl_26, tbl_27, tbl_28, tbl_29, tbl_30, tbl_31, tbl_32, tbl_33, tbl_34, tbl_35, tbl_36, tbl_37, tbl_38, W_top1, b_top1, W_top2, b_top2, W_top3)
    dense_ctx, ids, tbl_0, tbl_1, tbl_2, tbl_3, tbl_4, tbl_5, tbl_6, tbl_7, tbl_8, tbl_9, tbl_10, tbl_11, tbl_12, tbl_13, tbl_14, tbl_15, tbl_16, tbl_17, tbl_18, tbl_19, tbl_20, tbl_21, tbl_22, tbl_23, tbl_24, tbl_25, tbl_26, tbl_27, tbl_28, tbl_29, tbl_30, tbl_31, tbl_32, tbl_33, tbl_34, tbl_35, tbl_36, tbl_37, tbl_38, W_top1, b_top1, W_top2, b_top2, W_top3 = _rec_inputs()

    def _L0_rec_setup():
        import jax, jax.numpy as jnp
        import numpy as np
        B, F_FIELDS, D = (2048, 39, 64)
        key = jax.random.key(seed)
        x = jax.random.normal(key, (B, F_FIELDS, D), dtype=jnp.float32)
        return {'x': x}
    _L0_rec_all = _L0_rec_setup()
    _L0_rec_in = {k: v for k, v in _L0_rec_all.items() if k in ()}
    del _L0_rec_all
    return {'dense_ctx': dense_ctx, 'ids': ids, 'tbl_0': tbl_0, 'tbl_1': tbl_1, 'tbl_2': tbl_2, 'tbl_3': tbl_3, 'tbl_4': tbl_4, 'tbl_5': tbl_5, 'tbl_6': tbl_6, 'tbl_7': tbl_7, 'tbl_8': tbl_8, 'tbl_9': tbl_9, 'tbl_10': tbl_10, 'tbl_11': tbl_11, 'tbl_12': tbl_12, 'tbl_13': tbl_13, 'tbl_14': tbl_14, 'tbl_15': tbl_15, 'tbl_16': tbl_16, 'tbl_17': tbl_17, 'tbl_18': tbl_18, 'tbl_19': tbl_19, 'tbl_20': tbl_20, 'tbl_21': tbl_21, 'tbl_22': tbl_22, 'tbl_23': tbl_23, 'tbl_24': tbl_24, 'tbl_25': tbl_25, 'tbl_26': tbl_26, 'tbl_27': tbl_27, 'tbl_28': tbl_28, 'tbl_29': tbl_29, 'tbl_30': tbl_30, 'tbl_31': tbl_31, 'tbl_32': tbl_32, 'tbl_33': tbl_33, 'tbl_34': tbl_34, 'tbl_35': tbl_35, 'tbl_36': tbl_36, 'tbl_37': tbl_37, 'tbl_38': tbl_38, 'W_top1': W_top1, 'b_top1': b_top1, 'W_top2': W_top2, 'b_top2': b_top2, 'W_top3': W_top3}

def reference(dense_ctx, ids, tbl_0, tbl_1, tbl_2, tbl_3, tbl_4, tbl_5, tbl_6, tbl_7, tbl_8, tbl_9, tbl_10, tbl_11, tbl_12, tbl_13, tbl_14, tbl_15, tbl_16, tbl_17, tbl_18, tbl_19, tbl_20, tbl_21, tbl_22, tbl_23, tbl_24, tbl_25, tbl_26, tbl_27, tbl_28, tbl_29, tbl_30, tbl_31, tbl_32, tbl_33, tbl_34, tbl_35, tbl_36, tbl_37, tbl_38, W_top1, b_top1, W_top2, b_top2, W_top3):
    import jax
    import jax.numpy as jnp

    def _L0_rec_ref(x):
        import jax, jax.numpy as jnp
        import numpy as np
        B, F_FIELDS, D = (2048, 39, 64)
        F = x.shape[1]
        gram = jnp.einsum('bfd,bgd->bfg', x, x)
        row, col = jnp.triu_indices(F, k=1)
        return gram[:, row, col]
    e = jnp.stack([tbl_0[ids[:, 0]], tbl_1[ids[:, 1]], tbl_2[ids[:, 2]], tbl_3[ids[:, 3]], tbl_4[ids[:, 4]], tbl_5[ids[:, 5]], tbl_6[ids[:, 6]], tbl_7[ids[:, 7]], tbl_8[ids[:, 8]], tbl_9[ids[:, 9]], tbl_10[ids[:, 10]], tbl_11[ids[:, 11]], tbl_12[ids[:, 12]], tbl_13[ids[:, 13]], tbl_14[ids[:, 14]], tbl_15[ids[:, 15]], tbl_16[ids[:, 16]], tbl_17[ids[:, 17]], tbl_18[ids[:, 18]], tbl_19[ids[:, 19]], tbl_20[ids[:, 20]], tbl_21[ids[:, 21]], tbl_22[ids[:, 22]], tbl_23[ids[:, 23]], tbl_24[ids[:, 24]], tbl_25[ids[:, 25]], tbl_26[ids[:, 26]], tbl_27[ids[:, 27]], tbl_28[ids[:, 28]], tbl_29[ids[:, 29]], tbl_30[ids[:, 30]], tbl_31[ids[:, 31]], tbl_32[ids[:, 32]], tbl_33[ids[:, 33]], tbl_34[ids[:, 34]], tbl_35[ids[:, 35]], tbl_36[ids[:, 36]], tbl_37[ids[:, 37]], tbl_38[ids[:, 38]]], axis=1)
    z = _L0_rec_ref(e)
    z = z.reshape(z.shape[0], -1)
    h = jnp.concatenate([z, dense_ctx], axis=1)
    h = jnp.maximum(h @ W_top1 + b_top1, 0.0)
    h = jnp.maximum(h @ W_top2 + b_top2, 0.0)
    y = h @ W_top3
    return y

_drawn_inputs = setup_inputs


def setup_inputs(seed=0):
    import zlib

    import numpy as np

    out = dict(_drawn_inputs(seed))
    spreads = {'b_top1': (0.0, 0.1), 'b_top2': (0.0, 0.1)}
    factors = {'tbl_0': 2.712, 'tbl_29': 2.686}
    for name, (base, spread) in spreads.items():
        noise = np.random.default_rng([zlib.crc32(name.encode()), seed]).standard_normal(out[name].shape)
        drawn = base * np.exp(spread * noise) if base else spread * noise
        out[name] = jnp.asarray(drawn.astype(out[name].dtype))
    for name, factor in factors.items():
        out[name] = (out[name] * factor).astype(out[name].dtype)
    return out
```

```python
import concourse.bass as bass
from concourse import mybir
from contextlib import ExitStack

FIELDS = 39
DIM = 64
BATCH = 512
TILE = 128
TILES = BATCH // TILE
PAIRS = TILE // 2
GW = 2 * FIELDS
PER_BANK = 512 // GW
GRAM_BATCHES = -(-PAIRS // PER_BANK)
GROUP = 8
GROUPS = -(-FIELDS // GROUP)
DENSE = 16
H1, H2 = 512, 256
M1, M2 = H1 // 128, H2 // 128

CHUNKS = 7
BLOCKS = []
_at, _g = 0, FIELDS - 1
while _g > 0:
    _n = min(CHUNKS, _g)
    BLOCKS.append((_at, _g, _g - _n + 1, _n))
    _at, _g = _at + _g, _g - _n
DENSE_ROWS = 8
DENSE_AT = 128 - DENSE_ROWS
DENSE_CHUNK = BLOCKS[-1][3]
PAD_AT = 96
assert BLOCKS[-1][0] >= DENSE_AT and BLOCKS[-1][0] + BLOCKS[-1][1] <= 128


def slot_rows():
    rows = [[-1] * CHUNKS for _ in range(128)]
    for at, _, g0, n in BLOCKS:
        for c in range(n):
            g = g0 + c
            for f in range(g):
                rows[at + f][c] = f * FIELDS - f * (f + 1) // 2 + (g - f - 1)
    z = FIELDS * (FIELDS - 1) // 2
    for c in range(DENSE // DENSE_ROWS):
        for r in range(DENSE_ROWS):
            rows[DENSE_AT + r][DENSE_CHUNK + c] = z + c * DENSE_ROWS + r
    return rows


def group_fields(k):
    return range(GROUP * k, min(GROUP * k + GROUP, FIELDS))


def dlrm_kernel(nc, tables, ids, denseT, w1, b1, w2, b2, w3, eye, out):
    f32, i32 = mybir.dt.float32, mybir.dt.int32
    ACT = mybir.ActivationFunctionType
    ALU = mybir.AluOpType

    with ExitStack() as ctx:
        def sb(name, shape, dt=f32):
            return ctx.enter_context(nc.sbuf_tensor(name, shape, dt))

        def pb(name):
            return ctx.enter_context(nc.psum_tensor(name, [128, 512], f32))

        def sem(name):
            return ctx.enter_context(nc.semaphore(name))

        idx = sb("idx", [128, TILES * FIELDS], i32)
        ident = sb("ident", [128, 128])
        emb = sb("emb", [128, 2, FIELDS * DIM])
        embT = sb("embT", [128, TILE, FIELDS])
        grams = sb("grams", [GW, 2, GW, PAIRS])
        zT = sb("zT", [128, 2, CHUNKS, TILE])
        w1_sb = sb("w1_sb", [128, CHUNKS, H1])
        w2_sb = sb("w2_sb", [128, M1, H2])
        w3_sb = sb("w3_sb", [128, M2])
        b1_sb = sb("b1_sb", [128, M1])
        b2_sb = sb("b2_sb", [128, M2])
        h1 = sb("h1", [128, M1, TILE])
        h2 = sb("h2", [128, M2, TILE])
        y = sb("y", [1, BATCH])

        turn_ps = [pb(f"turn_ps{i}") for i in range(2)]
        gram_ps = [pb(f"gram_ps{i}") for i in range(2)]
        h1_ps = [pb(f"h1_ps{i}") for i in range(2)]
        h2_ps = pb("h2_ps")
        y_ps = pb("y_ps")

        ids_in = sem("ids_in")
        ident_in = sem("ident_in")
        w1_in = sem("w1_in")
        small_in = sem("small_in")
        zt_cleared = sem("zt_cleared")
        dense_in = [sem(f"dense_in{i}") for i in range(2)]
        gathered = [[sem(f"gathered{i}_{k}") for k in range(GROUPS)] for i in range(2)]
        turned = sem("turned")
        even_out = sem("even_out")
        odd_out = sem("odd_out")
        gram_done = sem("gram_done")
        gram_out = [sem(f"gram_out{i}") for i in range(2)]
        repacked = [sem(f"repacked{i}") for i in range(2)]
        l1_done = sem("l1_done")
        h1_out = sem("h1_out")
        l2_done = sem("l2_done")
        h2_out = sem("h2_out")
        l3_done = sem("l3_done")
        y_out = sem("y_out")
        stored = sem("stored")

        REPACKS = 2 * len(BLOCKS)
        BANK_BATCHES = [-(-GRAM_BATCHES // 2), GRAM_BATCHES // 2]

        def batch_pairs(q):
            return range(PER_BANK * q, min(PER_BANK * q + PER_BANK, PAIRS))

        block = ctx.enter_context(nc.Block())

        def repack(eng, t):
            i = t % 2
            for b in range(2):
                eng.wait_ge(gram_out[b], BANK_BATCHES[b] * (t + 1))
            if t >= 2:
                eng.wait_ge(l1_done, 2 * (t - 1))
            for at, rows, g0, n in BLOCKS:
                for s in range(2):
                    src = grams[FIELDS * s:FIELDS * s + rows, i, FIELDS * s + g0:FIELDS * s + g0 + n, :]
                    dst = zT[at:at + rows, i, 0:n, PAIRS * s:PAIRS * s + PAIRS]
                    eng.dma_start(dst, src).then_inc(repacked[i], 16)

        def load_dense(eng, t):
            for c in range(DENSE // DENSE_ROWS):
                eng.dma_start(zT[DENSE_AT:128, t % 2, DENSE_CHUNK + c, :],
                              denseT[DENSE_ROWS * c:DENSE_ROWS * (c + 1), TILE * t:TILE * (t + 1)])\
                   .then_inc(dense_in[t % 2], 16)

        @block.sync
        def _(sp):
            sp.dma_start(idx[:, :], ids).then_inc(ids_in, 16)
            sp.dma_start(ident[:, :], eye).then_inc(ident_in, 16)
            sp.dma_start(w1_sb[:, :, :], w1.rearrange("p (c n) -> p c n", c=CHUNKS)).then_inc(w1_in, 16)
            sp.dma_start(w2_sb[:, :, :], w2.rearrange("(k p) n -> p k n", p=128)).then_inc(small_in, 16)
            with nc.allow_non_contiguous_dma(reason="a few hundred words"):
                sp.dma_start(w3_sb[:, :], w3.rearrange("(k p) o -> p (k o)", p=128)).then_inc(small_in, 16)
                sp.dma_start(b1_sb[:, :], b1.rearrange("(k p) -> p k", p=128)).then_inc(small_in, 16)
                sp.dma_start(b2_sb[:, :], b2.rearrange("(k p) -> p k", p=128)).then_inc(small_in, 16)
            sp.wait_ge(zt_cleared, 1)
            for t in range(TILES):
                if t >= 2:
                    sp.wait_ge(l1_done, 2 * (t - 1))
                load_dense(sp, t)
                repack(sp, t)
            sp.wait_ge(y_out, TILES)
            sp.dma_start(out.rearrange("b o -> o b"), y[:, :]).then_inc(stored, 16)
            sp.wait_ge(stored, 16)

        @block.gpsimd
        def _(pool):
            pool.wait_ge(ids_in, 16)
            for t in range(TILES):
                for k in range(GROUPS):
                    if t >= 2:
                        pool.wait_ge(turned, GROUPS * (t - 2) + k + 1)
                    for f in group_fields(k):
                        pool.indirect_dma_start(
                            out=emb[:, t % 2, DIM * f:DIM * (f + 1)], out_offset=None, in_=tables[f],
                            in_offset=bass.IndirectOffsetOnAxis(ap=idx[:, t * FIELDS + f:t * FIELDS + f + 1], axis=0),
                        ).then_inc(gathered[t % 2][k], 16)

        def take_turned(eng_copy, eng, t, k, odd, done):
            n = GROUPS * t + k
            half = DIM * (t % 2)
            fields = [f for f in group_fields(k) if f % 2 == odd]
            if t >= 2 and k == 0:
                eng.wait_ge(gram_done, GRAM_BATCHES * (t - 1))
            eng.wait_ge(turned, n + 1)
            src = turn_ps[n % 2][DIM * odd:DIM * odd + DIM, 0:TILE * len(fields)]
            dst = embT[half:half + DIM, :, fields[0]:fields[-1] + 1:2]
            eng_copy(dst.rearrange("d b f -> d f b"),
                     src.rearrange("d (f b) -> d f b", b=TILE)).then_inc(done, 1)

        def take_grams(eng_copy, eng, t, bank):
            if t >= 2:
                eng.wait_ge(repacked[t % 2], 16 * REPACKS * (t // 2))
            for q in range(bank, GRAM_BATCHES, 2):
                pr = batch_pairs(q)
                eng.wait_ge(gram_done, GRAM_BATCHES * t + q + 1)
                src = gram_ps[bank][0:GW, 0:GW * len(pr)].rearrange("r (j n) -> r n j", n=GW)
                eng_copy(grams[:, t % 2, :, pr[0]:pr[-1] + 1], src).then_inc(gram_out[bank], 1)

        @block.vector
        def _(dve):
            nc.vector.memset(zT[PAD_AT:128, :, :, :], 0.0).then_inc(zt_cleared, 1)
            for t in range(TILES + 1):
                if t < TILES:
                    take_turned(nc.vector.tensor_copy, dve, t, 0, 0, even_out)
                if t >= 1:
                    take_grams(nc.vector.tensor_copy, dve, t - 1, 0)
                if t < TILES:
                    for k in range(1, GROUPS):
                        take_turned(nc.vector.tensor_copy, dve, t, k, 0, even_out)

        @block.scalar
        def _(act):
            def copy(dst, src):
                return nc.scalar.activation(dst, src, ACT.Copy)

            def mlp_outputs(t):
                if t == 0:
                    act.wait_ge(small_in, 16 * 4)
                for half in range(2):
                    act.wait_ge(l1_done, 2 * t + half + 1)
                    if t >= 1 and half == 0:
                        act.wait_ge(l2_done, t)
                    for m in (2 * half, 2 * half + 1):
                        ins = nc.scalar.activation(h1[:, m, :], h1_ps[half][:, TILE * (m % 2):TILE * (m % 2) + TILE],
                                                   ACT.Relu, bias=b1_sb[:, m:m + 1])
                    ins.then_inc(h1_out, 1)
                act.wait_ge(l2_done, t + 1)
                if t >= 1:
                    act.wait_ge(l3_done, t)
                for m in range(M2):
                    ins = nc.scalar.activation(h2[:, m, :], h2_ps[:, TILE * m:TILE * m + TILE],
                                               ACT.Relu, bias=b2_sb[:, m:m + 1])
                ins.then_inc(h2_out, 1)
                act.wait_ge(l3_done, t + 1)
                copy(y[:, TILE * t:TILE * (t + 1)], y_ps[0:1, 0:TILE]).then_inc(y_out, 1)

            for t in range(TILES + 1):
                if t < TILES:
                    take_turned(copy, act, t, 0, 1, odd_out)
                if t >= 1:
                    take_grams(copy, act, t - 1, 1)
                if t < TILES:
                    take_turned(copy, act, t, 1, 1, odd_out)
                    take_turned(copy, act, t, 2, 1, odd_out)
                if t >= 1:
                    mlp_outputs(t - 1)
                if t < TILES:
                    for k in range(3, GROUPS):
                        take_turned(copy, act, t, k, 1, odd_out)

        @block.tensor
        def _(pe):
            def turn(t, k):
                n = GROUPS * t + k
                fields = group_fields(k)
                pe.wait_ge(gathered[t % 2][k], 16 * len(fields) * (t // 2 + 1))
                if n >= 2:
                    pe.wait_ge(even_out, n - 1)
                    pe.wait_ge(odd_out, n - 1)
                for j, f in enumerate(fields[::2]):
                    w = DIM * min(2, FIELDS - f)
                    ins = nc.tensor.transpose(turn_ps[n % 2][0:w, TILE * j:TILE * (j + 1)],
                                              emb[:, t % 2, DIM * f:DIM * f + w], ident[:, :])
                ins.then_inc(turned, 1)

            def gram(t):
                half = DIM * (t % 2)
                pe.wait_ge(even_out, GROUPS * (t + 1))
                pe.wait_ge(odd_out, GROUPS * (t + 1))
                for q in range(GRAM_BATCHES):
                    before = BANK_BATCHES[q % 2] * t + q // 2
                    if before:
                        pe.wait_ge(gram_out[q % 2], before)
                    for n, j in enumerate(batch_pairs(q)):
                        both = embT[half:half + DIM, 2 * j:2 * j + 2, :].rearrange("d b f -> d (b f)")
                        ins = nc.tensor.matmul(gram_ps[q % 2][0:GW, GW * n:GW * (n + 1)], both, both,
                                               start=True, stop=True)
                    ins.then_inc(gram_done, 1)

            def mlp(t):
                i = t % 2
                if t == 0:
                    pe.wait_ge(w1_in, 16)
                    pe.wait_ge(small_in, 16 * 4)
                pe.wait_ge(dense_in[i], 16 * (DENSE // DENSE_ROWS) * (t // 2 + 1))
                pe.wait_ge(repacked[i], 16 * REPACKS * (t // 2 + 1))
                for half in range(2):
                    if t >= 1:
                        pe.wait_ge(h1_out, 2 * (t - 1) + half + 1)
                    for m in (2 * half, 2 * half + 1):
                        for c in range(CHUNKS):
                            ins = nc.tensor.matmul(h1_ps[half][:, TILE * (m % 2):TILE * (m % 2) + TILE],
                                                   w1_sb[:, c, 128 * m:128 * (m + 1)], zT[:, i, c, :],
                                                   start=(c == 0), stop=(c == CHUNKS - 1))
                    ins.then_inc(l1_done, 1)
                if t >= 1:
                    pe.wait_ge(h2_out, t)
                pe.wait_ge(h1_out, 2 * (t + 1))
                for m in range(M2):
                    for k in range(M1):
                        ins = nc.tensor.matmul(h2_ps[:, TILE * m:TILE * m + TILE],
                                               w2_sb[:, k, 128 * m:128 * (m + 1)], h1[:, k, :],
                                               start=(k == 0), stop=(k == M1 - 1))
                ins.then_inc(l2_done, 1)
                if t >= 1:
                    pe.wait_ge(y_out, t)
                pe.wait_ge(h2_out, t + 1)
                for k in range(M2):
                    ins = nc.tensor.matmul(y_ps[0:1, 0:TILE], w3_sb[:, k:k + 1], h2[:, k, :],
                                           start=(k == 0), stop=(k == M2 - 1))
                ins.then_inc(l3_done, 1)

            pe.wait_ge(ident_in, 16)
            for t in range(TILES + 1):
                if t < TILES:
                    turn(t, 0)
                if t >= 1:
                    gram(t - 1)
                if t < TILES:
                    turn(t, 1)
                    turn(t, 2)
                if t >= 1:
                    mlp(t - 1)
                if t < TILES:
                    for k in range(3, GROUPS):
                        turn(t, k)


def kernel(**inputs):
    import numpy as np
    import concourse.bacc as bacc
    from concourse.bass_utils import run_bass_kernel_spmd as run

    nc = bacc.Bacc("TRN2", target_bir_lowering=False, num_devices=1)
    arrays = {}

    def dram(name, a):
        a = np.ascontiguousarray(a)
        arrays[name] = a
        return nc.dram_tensor(name, a.shape, mybir.dt.from_np(a.dtype), kind="ExternalInput").ap()

    tables = [dram(f"tbl_{f}", np.asarray(inputs[f"tbl_{f}"])) for f in range(FIELDS)]
    ids = np.asarray(inputs["ids"]).reshape(TILES, 2, PAIRS, FIELDS).transpose(2, 1, 0, 3)
    w1 = np.asarray(inputs["W_top1"])
    rows = np.array(slot_rows())
    w1_slots = np.concatenate([w1, np.zeros((1, H1), w1.dtype)])[rows]
    args = dict(
        ids=dram("ids", ids.reshape(TILE, TILES * FIELDS)),
        denseT=dram("denseT", np.asarray(inputs["dense_ctx"]).T),
        w1=dram("w1", w1_slots.reshape(128, CHUNKS * H1)),
        b1=dram("b1", np.asarray(inputs["b_top1"])),
        w2=dram("w2", np.asarray(inputs["W_top2"])),
        b2=dram("b2", np.asarray(inputs["b_top2"])),
        w3=dram("w3", np.asarray(inputs["W_top3"])),
        eye=dram("eye", np.eye(128, dtype=np.float32)),
    )
    out = nc.dram_tensor("out_y", (BATCH, 1), mybir.dt.float32, kind="ExternalOutput").ap()
    dlrm_kernel(nc, tables, out=out, **args)
    r = run(nc, [arrays], core_ids=[0])
    return r.results[0]["out_y"]
```

```python
import concourse.bass as bass
from concourse import mybir
from contextlib import ExitStack

FIELDS = 39
DIM = 64
BATCH = 512
TILE = 128
TILES = BATCH // TILE
PAIRS = TILE // 2
GW = 2 * FIELDS
PER_BANK = 512 // GW
GRAM_BATCHES = -(-PAIRS // PER_BANK)
GRAM_BANKS = 3
GROUP = 8
GROUPS = -(-FIELDS // GROUP)
DENSE = 16
H1, H2 = 512, 256
M1, M2 = H1 // 128, H2 // 128

TP = 125
ROWS_OF = [125000, 1250, 125000, 1250, 12500, 1000, 1000, 1000, 125000, 1250, 12500, 12500, 1250,
           1250, 1000, 12500, 1250, 12500, 1000, 1000, 1250, 1000, 1250, 1250, 1250, 1250,
           12500, 1000, 12500, 1250, 1250, 1000, 1000, 1250, 1250, 1250, 1000, 1250, 1000]
GATHER_FIELDS = 26
_small_first = sorted(range(FIELDS), key=lambda f: (ROWS_OF[f], f))
ONE_HOT = _small_first[:FIELDS - GATHER_FIELDS]
GATHERED = [f for f in range(FIELDS) if f not in ONE_HOT]
ORDER = GATHERED + ONE_HOT
FIRST_HOT = len(GATHERED)
GATHER_GROUPS = -(-FIRST_HOT // GROUP)
KC = [ROWS_OF[f] // TP for f in ONE_HOT]
KC_MAX = max(KC)
KC_KINDS = sorted(set(KC))
assert all(ROWS_OF[f] % TP == 0 for f in ONE_HOT)
PARTS = 3
PARTS_W = PARTS * DIM
RING = 5
AHEAD = 3
IDS_LOT = 4

CHUNKS = 7
BLOCKS = []
_at, _g = 0, FIELDS - 1
while _g > 0:
    _n = min(CHUNKS, _g)
    BLOCKS.append((_at, _g, _g - _n + 1, _n))
    _at, _g = _at + _g, _g - _n
DENSE_ROWS = 8
DENSE_AT = 128 - DENSE_ROWS
DENSE_CHUNK = BLOCKS[-1][3]
PAD_AT = 96
REPACKS = 2 * len(BLOCKS)
assert BLOCKS[-1][0] >= DENSE_AT and BLOCKS[-1][0] + BLOCKS[-1][1] <= 128


def zt_rows():
    rows = [[-1] * CHUNKS for _ in range(128)]
    for at, _, g0, n in BLOCKS:
        for c in range(n):
            for f in range(g0 + c):
                a, b = sorted((ORDER[f], ORDER[g0 + c]))
                rows[at + f][c] = a * FIELDS - a * (a + 1) // 2 + (b - a - 1)
    z = FIELDS * (FIELDS - 1) // 2
    for c in range(DENSE // DENSE_ROWS):
        for r in range(DENSE_ROWS):
            rows[DENSE_AT + r][DENSE_CHUNK + c] = z + c * DENSE_ROWS + r
    return rows


HOTS = len(ONE_HOT)


def hots(first, last):
    return [("hot", s) for s in range(first, last + 1)]


STEPS = (hots(0, 2) + [("turn", 0, 0)] + hots(3, 4) + [("turn", 0, 1)] + hots(5, 7)
         + [("turn", 0, 2), ("turn", 0, 3)] + hots(8, 10) + [("turn", 1, 0)] + hots(11, HOTS - 1)
         + [("turn", 0, 4), ("gram", 0), ("turn", 1, 1), ("turn", 1, 3), ("turn", 1, 4), ("turn", 1, 2), ("gram", 1)]
         + [("turn", 2, 4), ("turn", 2, 0), ("l1", 0)]
         + [("turn", 2, 1), ("l2", 0), ("turn", 2, 2), ("l3", 0), ("turn", 2, 3), ("gram", 2), ("l1", 1)]
         + [("turn", 3, 4), ("l2", 1), ("turn", 3, 0), ("l3", 1), ("turn", 3, 1), ("l1", 2)]
         + [("turn", 3, 2), ("turn", 3, 3), ("gram", 3), ("l2", 2), ("l3", 2), ("l1", 3), ("l2", 3), ("l3", 3)])
ZERO_AFTER, W1_AFTER, W2_AFTER = (8, 11), 10, 12
TURNS = [step[1:] for step in STEPS if step[0] == "turn"]
assert sorted(TURNS) == [(t, k) for t in range(TILES) for k in range(GROUPS)]
assert [s[1] for s in STEPS if s[0] == "hot"] == list(range(HOTS))


def group_slots(k):
    return range(GROUP * k, min(GROUP * k + GROUP, FIELDS))


def gathered_slots(k):
    return range(GROUP * k, min(GROUP * k + GROUP, FIRST_HOT))


def evens_on_dve(t):
    return t >= 2


def even_count(n):
    return sum(evens_on_dve(t) == evens_on_dve(TURNS[n][0]) for t, _ in TURNS[:n + 1])


def last_turn(t):
    return max(n for n, turn in enumerate(TURNS) if turn[0] == t)


def gram_count(e, n):
    return (n + 1 - e) // 2


def batch_pairs(q):
    return range(PER_BANK * q, min(PER_BANK * q + PER_BANK, PAIRS))


def dlrm_kernel(nc, tables, ids, ids_hot, denseT, w1, b1, w2, b2, w3, eye, zeros, out):
    f32, i32 = mybir.dt.float32, mybir.dt.int32
    bf16, f16 = mybir.dt.bfloat16, mybir.dt.float16
    ACT = mybir.ActivationFunctionType
    ALU = mybir.AluOpType

    with ExitStack() as ctx:
        def sb(name, shape, dt=f32):
            return ctx.enter_context(nc.sbuf_tensor(name, shape, dt))

        def pb(name):
            return ctx.enter_context(nc.psum_tensor(name, [128, 512], f32))

        def sem(name):
            return ctx.enter_context(nc.semaphore(name))

        idx = sb("idx", [128, TILES * FIRST_HOT], i32)
        ident = sb("ident", [128, 128])
        emb = sb("emb", [128, TILES, FIELDS * DIM])
        embT = sb("embT", [128, 2, TILE * FIELDS])
        shared = sb("shared", [128, 2 * GW * PAIRS])
        grams = shared[0:GW, :].rearrange("p (i n j) -> p i n j", i=2, n=GW)
        zT = sb("zT", [128, 2, CHUNKS, TILE])
        w1_sb = sb("w1_sb", [128, CHUNKS, H1])
        w2_sb = sb("w2_sb", [128, M1, H2])
        w3_sb = sb("w3_sb", [128, M2])
        b1_sb = sb("b1_sb", [128, M1])
        b2_sb = sb("b2_sb", [128, M2])
        h1 = sb("h1", [128, M1, TILE])
        h2 = sb("h2", [128, M2, TILE])
        y = sb("y", [1, BATCH])
        ids_all = sb("ids_all", [TP, 2, IDS_LOT, BATCH], i32)
        first_row = sb("first_row", [TP, len(KC_KINDS), 2])
        chunk_of = sb("chunk_of", [TP, AHEAD, 2, BATCH], f16)
        hot = sb("hot", [TP, AHEAD, KC_MAX, BATCH], bf16)
        parts_words = shared[0:TP, 0:RING * KC_MAX * PARTS_W]
        parts = parts_words.rearrange("p (i k a d) -> p i k a d", i=RING, k=KC_MAX, a=PARTS)
        halves = parts_words.bitcast(bf16)
        upper = halves.rearrange("p (i k a d two) -> p i k a d two", i=RING, k=KC_MAX, a=PARTS, two=2)
        upper_row = halves.rearrange("p (i k n two) -> p i k n two", i=RING, k=KC_MAX, two=2)

        turn_ps = [pb(f"turn_ps{i}") for i in range(2)]
        gram_ps = [pb(f"gram_ps{i}") for i in range(GRAM_BANKS)]
        wide_ps = [pb(f"wide_ps{i}") for i in range(2)]
        head_ps = pb("head_ps")
        h2_ps = head_ps[:, 0:M2 * TILE]
        y_ps = head_ps[0:1, M2 * TILE:(M2 + 1) * TILE]

        ids_in = sem("ids_in")
        ids_lot_in = [sem(f"ids_lot_in{i}") for i in range(-(-HOTS // IDS_LOT))]
        ident_in = sem("ident_in")
        w1_in = sem("w1_in")
        small_in = sem("small_in")
        table_in = [sem(f"table_in{i}") for i in range(RING)]
        zt_cleared = sem("zt_cleared")
        first_row_made = sem("first_row_made")
        chunk_of_made = sem("chunk_of_made")
        second_made = sem("second_made")
        zeros_in = sem("zeros_in")
        parts_made = sem("parts_made")
        hot_made = sem("hot_made")
        hot_done = sem("hot_done")
        hot_out = sem("hot_out")
        dense_in = [sem(f"dense_in{i}") for i in range(2)]
        gathered = [[sem(f"gathered{t}_{k}") for k in range(GATHER_GROUPS)] for t in range(TILES)]
        turned = sem("turned")
        even_out = {True: sem("even_out_dve"), False: sem("even_out_act")}
        odd_out = sem("odd_out")
        gram_done = sem("gram_done")
        gram_out = [sem("gram_out_dve"), sem("gram_out_act")]
        repacked = [sem(f"repacked{i}") for i in range(2)]
        repacked_by_pool = sem("repacked_by_pool")
        l1_done = sem("l1_done")
        h1_out = sem("h1_out")
        l2_done = sem("l2_done")
        h2_out = sem("h2_out")
        l3_done = sem("l3_done")
        y_out = sem("y_out")
        stored = sem("stored")

        block = ctx.enter_context(nc.Block())

        def repack(eng, t, s, done):
            if t >= 2:
                eng.wait_ge(l1_done, 2 * (t - 1))
            for e in range(2):
                eng.wait_ge(gram_out[e], gram_count(e, GRAM_BATCHES * (t + 1)))
            for at, rows, g0, n in BLOCKS:
                src = grams[FIELDS * s:FIELDS * s + rows, t % 2, FIELDS * s + g0:FIELDS * s + g0 + n, :]
                eng.dma_start(zT[at:at + rows, t % 2, 0:n, PAIRS * s:PAIRS * (s + 1)], src).then_inc(done, 16)

        def load_ids_lot(eng, n):
            lot = slice(IDS_LOT * n, min(IDS_LOT * n + IDS_LOT, HOTS))
            count = lot.stop - lot.start
            if n >= 2:
                eng.wait_ge(chunk_of_made, IDS_LOT * (n - 1))
            src = ids_hot[lot, :].rearrange("(o s) b -> o (s b)", o=1).to_broadcast([TP, count * BATCH])
            eng.dma_start(ids_all[:, n % 2, 0:count, :].rearrange("p s b -> p (s b)"), src).then_inc(ids_lot_in[n], 16)

        @block.sync
        def _(sp):
            def load_table(s):
                if s >= RING:
                    sp.wait_ge(hot_done, 2 * (s - RING + 1))
                sp.dma_start(parts[:, s % RING, 0:KC[s], 0, :],
                             tables[ONE_HOT[s]].rearrange("(p k) d -> p k d", k=KC[s])).then_inc(table_in[s % RING], 16)

            sp.dma_start(idx[:, :], ids).then_inc(ids_in, 16)
            load_table(0)
            sp.dma_start(ident[:, :], eye).then_inc(ident_in, 16)
            load_table(1)
            load_table(2)
            load_ids_lot(sp, 1)
            for s in range(3, HOTS):
                if s % IDS_LOT == IDS_LOT - 1 and IDS_LOT < s < HOTS - 1:
                    load_ids_lot(sp, (s + 1) // IDS_LOT)
                load_table(s)
                if s in ZERO_AFTER:
                    i = ZERO_AFTER.index(s)
                    sp.dma_start(embT[DIM:128, i, :],
                                 zeros.rearrange("(o n) -> o n", o=1).to_broadcast([128 - DIM, TILE * FIELDS])).then_inc(zeros_in, 16)
                if s == W1_AFTER:
                    sp.dma_start(w1_sb[:, :, :], w1.rearrange("p (c n) -> p c n", c=CHUNKS)).then_inc(w1_in, 16)
                if s == W2_AFTER:
                    sp.dma_start(w2_sb[:, :, :], w2.rearrange("(k p) n -> p k n", p=128)).then_inc(small_in, 16)
                    with nc.allow_non_contiguous_dma(reason="a few hundred words"):
                        sp.dma_start(w3_sb[:, :], w3.rearrange("(k p) o -> p (k o)", p=128)).then_inc(small_in, 16)
                        sp.dma_start(b1_sb[:, :], b1.rearrange("(k p) -> p k", p=128)).then_inc(small_in, 16)
                        sp.dma_start(b2_sb[:, :], b2.rearrange("(k p) -> p k", p=128)).then_inc(small_in, 16)
            sp.wait_ge(zt_cleared, 1)
            for t in range(TILES):
                i = t % 2
                if t >= 2:
                    sp.wait_ge(l1_done, 2 * (t - 1))
                for c in range(DENSE // DENSE_ROWS):
                    sp.dma_start(zT[DENSE_AT:128, i, DENSE_CHUNK + c, :],
                                 denseT[DENSE_ROWS * c:DENSE_ROWS * (c + 1), TILE * t:TILE * (t + 1)])\
                      .then_inc(dense_in[i], 16)
                repack(sp, t, 0, repacked[i])
                if t < TILES - 1:
                    repack(sp, t, 1, repacked[i])
            sp.wait_ge(y_out, TILES)
            sp.dma_start(out.rearrange("b o -> o b"), y[:, :]).then_inc(stored, 16)
            sp.wait_ge(stored, 16)

        @block.gpsimd
        def _(pool):
            for i, kc in enumerate(KC_KINDS):
                ins = pool.iota(first_row[:, i, :], [[-(kc // 2), 2]], base=0, channel_multiplier=-kc,
                                allow_small_or_imprecise_dtypes=True)
            ins.then_inc(first_row_made, 1)
            pool.wait_ge(ids_in, 16)
            for t in range(TILES):
                for k in range(GATHER_GROUPS):
                    for f in gathered_slots(k):
                        at = t * FIRST_HOT + f
                        pool.indirect_dma_start(
                            out=emb[:, t, DIM * f:DIM * (f + 1)], out_offset=None, in_=tables[ORDER[f]],
                            in_offset=bass.IndirectOffsetOnAxis(ap=idx[:, at:at + 1], axis=0),
                        ).then_inc(gathered[t][k], 16)

            pool.wait_ge(zt_cleared, 1)
            repack(pool, TILES - 1, 1, repacked_by_pool)

        def take_turned(copy, eng, t, k, odd, done):
            n = TURNS.index((t, k))
            slots = [f for f in group_slots(k) if f % 2 == odd]
            if t >= 2:
                eng.wait_ge(gram_done, GRAM_BATCHES * (t - 1))
            eng.wait_ge(turned, n + 1)
            src = turn_ps[n % 2][DIM * odd:DIM * odd + DIM, 0:TILE * len(slots)]
            dst = embT[0:DIM, t % 2, :].rearrange("d (b f) -> d f b", f=FIELDS)[:, slots[0]:slots[-1] + 1:2, :]
            copy(dst, src.rearrange("d (f b) -> d f b", b=TILE)).then_inc(done, 1)

        def take_grams(copy, eng, t, e):
            if t >= 2:
                eng.wait_ge(repacked[t % 2], 16 * REPACKS * (t // 2))
            for q in range(GRAM_BATCHES):
                n = GRAM_BATCHES * t + q
                if n % 2 != e:
                    continue
                pr = batch_pairs(q)
                eng.wait_ge(gram_done, n + 1)
                src = gram_ps[n % GRAM_BANKS][0:GW, 0:GW * len(pr)].rearrange("r (j n) -> r n j", n=GW)
                copy(grams[:, t % 2, :, pr[0]:pr[-1] + 1], src).then_inc(gram_out[e], 1)

        @block.vector
        def _(dve):
            def prepare_hot(s):
                i, kc = s % RING, KC[s]
                dve.wait_ge(table_in[i], 16 * (s // RING + 1))
                nc.vector.tensor_tensor(parts[:, i, 0:kc, 1, :], parts[:, i, 0:kc, 0, :], upper[:, i, 0:kc, 0, :, 1],
                                        ALU.subtract).then_inc(second_made, 1)
                dve.wait_ge(chunk_of_made, s + 1)
                if s >= AHEAD:
                    dve.wait_ge(hot_done, 2 * (s - AHEAD + 1))
                for k in range(kc // 2):
                    ins = nc.vector.tensor_scalar(hot[:, s % AHEAD, k:kc:kc // 2, :], chunk_of[:, s % AHEAD, :, :],
                                                  float(k), None, ALU.is_equal)
                ins.then_inc(hot_made, 1)
                dve.wait_ge(second_made, s + 1)
                nc.vector.tensor_tensor(parts[:, i, 0:kc, 2, :], parts[:, i, 0:kc, 1, :], upper[:, i, 0:kc, 1, :, 1],
                                        ALU.subtract).then_inc(parts_made, 1)

            def sum_hot(s):
                slot = FIRST_HOT + s
                for half in range(2):
                    dve.wait_ge(hot_done, 2 * s + half + 1)
                    src = wide_ps[half][:, 0:2 * PARTS_W].rearrange("b (t a d) -> b t d a", t=2, a=PARTS)
                    nc.vector.tensor_reduce(emb[:, 2 * half:2 * half + 2, DIM * slot:DIM * (slot + 1)], src,
                                            op=ALU.add, axis=mybir.AxisListType.X).then_inc(hot_out, 1)

            for step in STEPS:
                if step[0] == "hot":
                    prepare_hot(step[1])
                    if step[1] == 0:
                        nc.vector.memset(zT[PAD_AT:128, :, :, :], 0.0).then_inc(zt_cleared, 1)
                    if step[1] >= 1:
                        sum_hot(step[1] - 1)
                    if step[1] == HOTS - 1:
                        sum_hot(step[1])
                elif step[0] == "turn" and evens_on_dve(step[1]):
                    take_turned(nc.vector.tensor_copy, dve, step[1], step[2], 0, even_out[True])
                elif step[0] == "gram":
                    take_grams(nc.vector.tensor_copy, dve, step[1], 0)

        @block.scalar
        def _(act):
            def copy(dst, src):
                return nc.scalar.activation(dst, src, ACT.Copy)

            def place_ids(s):
                kind = KC_KINDS.index(KC[s])
                if s % IDS_LOT == 0:
                    act.wait_ge(ids_lot_in[s // IDS_LOT], 16)
                if s >= AHEAD:
                    act.wait_ge(hot_made, s - AHEAD + 1)
                for half in range(2):
                    ins = nc.scalar.activation(chunk_of[:, s % AHEAD, half, :], ids_all[:, s // IDS_LOT % 2, s % IDS_LOT, :],
                                               ACT.Identity, bias=first_row[:, kind, half:half + 1])
                ins.then_inc(chunk_of_made, 1)

            def take_l1(t):
                if t == 0:
                    act.wait_ge(small_in, 16 * 4)
                else:
                    act.wait_ge(l2_done, t)
                for half in range(2):
                    act.wait_ge(l1_done, 2 * t + half + 1)
                    for m in (2 * half, 2 * half + 1):
                        ins = nc.scalar.activation(h1[:, m, :], wide_ps[half][:, TILE * (m % 2):TILE * (m % 2) + TILE],
                                                   ACT.Relu, bias=b1_sb[:, m:m + 1])
                    ins.then_inc(h1_out, 1)

            def take_l2(t):
                act.wait_ge(l2_done, t + 1)
                if t >= 1:
                    act.wait_ge(l3_done, t)
                for m in range(M2):
                    ins = nc.scalar.activation(h2[:, m, :], h2_ps[:, TILE * m:TILE * m + TILE],
                                               ACT.Relu, bias=b2_sb[:, m:m + 1])
                ins.then_inc(h2_out, 1)

            def take_l3(t):
                act.wait_ge(l3_done, t + 1)
                copy(y[:, TILE * t:TILE * (t + 1)], y_ps).then_inc(y_out, 1)

            load_ids_lot(act, 0)
            act.wait_ge(first_row_made, 1)
            nc.scalar.activation(y[:, 0:1], first_row[0:1, 0, 0:1], ACT.Identity)
            for s in range(AHEAD):
                place_ids(s)
            for step in STEPS:
                if step[0] == "hot":
                    if step[1] + AHEAD < HOTS:
                        place_ids(step[1] + AHEAD)
                elif step[0] == "turn":
                    t, k = step[1:]
                    if not evens_on_dve(t):
                        take_turned(copy, act, t, k, 0, even_out[False])
                    take_turned(copy, act, t, k, 1, odd_out)
                elif step[0] == "gram":
                    take_grams(copy, act, step[1], 1)
                elif step[0] == "l1":
                    take_l1(step[1])
                elif step[0] == "l2":
                    take_l2(step[1])
                else:
                    take_l3(step[1])

        @block.tensor
        def _(pe):
            def look_up(s):
                i, kc = s % RING, KC[s]
                pe.wait_ge(hot_made, s + 1)
                pe.wait_ge(parts_made, s + 1)
                for t in range(TILES):
                    if s >= 1 and t % 2 == 0:
                        pe.wait_ge(hot_out, 2 * (s - 1) + t // 2 + 1)
                    for k in range(kc):
                        ins = nc.tensor.matmul(wide_ps[t // 2][:, PARTS_W * (t % 2):PARTS_W * (t % 2 + 1)],
                                               hot[:, s % AHEAD, k, TILE * t:TILE * (t + 1)], upper_row[:, i, k, :, 1],
                                               start=(k == 0), stop=(k == kc - 1))
                    if t % 2:
                        ins.then_inc(hot_done, 1)

            def turn(t, k):
                n = TURNS.index((t, k))
                slots = group_slots(k)
                if slots[0] < FIRST_HOT:
                    pe.wait_ge(gathered[t][k], 16 * len(gathered_slots(k)))
                if slots[-1] >= FIRST_HOT:
                    pe.wait_ge(hot_out, 2 * (slots[-1] - FIRST_HOT) + t // 2 + 1)
                if n >= 2:
                    pe.wait_ge(even_out[evens_on_dve(TURNS[n - 2][0])], even_count(n - 2))
                    pe.wait_ge(odd_out, n - 1)
                for j, f in enumerate(slots[::2]):
                    w = DIM * min(2, FIELDS - f)
                    ins = nc.tensor.transpose(turn_ps[n % 2][0:w, TILE * j:TILE * (j + 1)],
                                              emb[:, t, DIM * f:DIM * f + w], ident[:, :])
                ins.then_inc(turned, 1)

            def gram(t):
                n = last_turn(t)
                pe.wait_ge(even_out[evens_on_dve(t)], even_count(n))
                pe.wait_ge(odd_out, n + 1)
                if t == 0:
                    pe.wait_ge(zeros_in, 32)
                for q in range(GRAM_BATCHES):
                    n = GRAM_BATCHES * t + q
                    if n >= GRAM_BANKS:
                        last = n - GRAM_BANKS
                        pe.wait_ge(gram_out[last % 2], gram_count(last % 2, last + 1))
                    for c, j in enumerate(batch_pairs(q)):
                        pair = embT[:, t % 2, GW * j:GW * (j + 1)]
                        ins = nc.tensor.matmul(gram_ps[n % GRAM_BANKS][0:GW, GW * c:GW * (c + 1)], pair, pair,
                                               start=True, stop=True)
                    ins.then_inc(gram_done, 1)

            def layer1(t):
                i = t % 2
                if t == 0:
                    pe.wait_ge(w1_in, 16)
                    pe.wait_ge(small_in, 16 * 4)
                    pe.wait_ge(hot_out, 2 * HOTS)
                pe.wait_ge(dense_in[i], 16 * (DENSE // DENSE_ROWS) * (t // 2 + 1))
                if t < TILES - 1:
                    pe.wait_ge(repacked[i], 16 * REPACKS * (t // 2 + 1))
                else:
                    pe.wait_ge(repacked[i], 16 * (REPACKS * (t // 2) + len(BLOCKS)))
                    pe.wait_ge(repacked_by_pool, 16 * len(BLOCKS))
                for half in range(2):
                    if t >= 1:
                        pe.wait_ge(h1_out, 2 * (t - 1) + half + 1)
                    for m in (2 * half, 2 * half + 1):
                        for c in range(CHUNKS):
                            ins = nc.tensor.matmul(wide_ps[half][:, TILE * (m % 2):TILE * (m % 2) + TILE],
                                                   w1_sb[:, c, 128 * m:128 * (m + 1)], zT[:, i, c, :],
                                                   start=(c == 0), stop=(c == CHUNKS - 1))
                    ins.then_inc(l1_done, 1)

            def layer2(t):
                if t >= 1:
                    pe.wait_ge(y_out, t)
                pe.wait_ge(h1_out, 2 * (t + 1))
                for m in range(M2):
                    for k in range(M1):
                        ins = nc.tensor.matmul(h2_ps[:, TILE * m:TILE * m + TILE],
                                               w2_sb[:, k, 128 * m:128 * (m + 1)], h1[:, k, :],
                                               start=(k == 0), stop=(k == M1 - 1))
                ins.then_inc(l2_done, 1)

            def layer3(t):
                pe.wait_ge(h2_out, t + 1)
                for k in range(M2):
                    ins = nc.tensor.matmul(y_ps, w3_sb[:, k:k + 1], h2[:, k, :],
                                           start=(k == 0), stop=(k == M2 - 1))
                ins.then_inc(l3_done, 1)

            pe.wait_ge(ident_in, 16)
            for step in STEPS:
                if step[0] == "hot":
                    look_up(step[1])
                elif step[0] == "turn":
                    turn(step[1], step[2])
                elif step[0] == "gram":
                    gram(step[1])
                elif step[0] == "l1":
                    layer1(step[1])
                elif step[0] == "l2":
                    layer2(step[1])
                else:
                    layer3(step[1])


def kernel(**inputs):
    import numpy as np
    import concourse.bacc as bacc
    from concourse.bass_utils import run_bass_kernel_spmd as run

    nc = bacc.Bacc("TRN2", target_bir_lowering=False, num_devices=1)
    arrays = {}

    def dram(name, a):
        a = np.ascontiguousarray(a)
        arrays[name] = a
        return nc.dram_tensor(name, a.shape, mybir.dt.from_np(a.dtype), kind="ExternalInput").ap()

    tables = [dram(f"tbl_{f}", np.asarray(inputs[f"tbl_{f}"])) for f in range(FIELDS)]
    ids = np.asarray(inputs["ids"]).reshape(TILES, 2, PAIRS, FIELDS).transpose(0, 2, 1, 3).reshape(BATCH, FIELDS)
    w1 = np.asarray(inputs["W_top1"])
    w1_rows = np.concatenate([w1, np.zeros((1, H1), w1.dtype)])[np.array(zt_rows())]
    args = dict(
        ids=dram("ids", ids[:, GATHERED].reshape(TILES, TILE, FIRST_HOT).transpose(1, 0, 2).reshape(TILE, -1)),
        ids_hot=dram("ids_hot", ids[:, ONE_HOT].T),
        denseT=dram("denseT", np.asarray(inputs["dense_ctx"]).T),
        w1=dram("w1", w1_rows.reshape(128, CHUNKS * H1)),
        b1=dram("b1", np.asarray(inputs["b_top1"])),
        w2=dram("w2", np.asarray(inputs["W_top2"])),
        b2=dram("b2", np.asarray(inputs["b_top2"])),
        w3=dram("w3", np.asarray(inputs["W_top3"])),
        eye=dram("eye", np.eye(128, dtype=np.float32)),
        zeros=dram("zeros", np.zeros(TILE * FIELDS, np.float32)),
    )
    out = nc.dram_tensor("out_y", (BATCH, 1), mybir.dt.float32, kind="ExternalOutput").ap()
    dlrm_kernel(nc, tables, out=out, **args)
    r = run(nc, [arrays], core_ids=[0])
    return r.results[0]["out_y"]
```

```python
import concourse.bass as bass
from concourse import mybir
from contextlib import ExitStack

FIELDS = 39
DIM = 64
BATCH = 512
TILE = 128
TILES = BATCH // TILE
PAIRS = TILE // 2
GW = 2 * FIELDS
PER_BANK = 512 // GW
GRAM_BATCHES = -(-PAIRS // PER_BANK)
GRAM_BANKS = 3
GROUP = 8
GROUPS = -(-FIELDS // GROUP)
DENSE = 16
H1, H2 = 512, 256
M1, M2 = H1 // 128, H2 // 128

TP = 125
ROWS_OF = [125000, 1250, 125000, 1250, 12500, 1000, 1000, 1000, 125000, 1250, 12500, 12500, 1250,
           1250, 1000, 12500, 1250, 12500, 1000, 1000, 1250, 1000, 1250, 1250, 1250, 1250,
           12500, 1000, 12500, 1250, 1250, 1000, 1000, 1250, 1250, 1250, 1000, 1250, 1000]
GATHER_FIELDS = 22
_small_first = sorted(range(FIELDS), key=lambda f: (ROWS_OF[f], f))
ONE_HOT = _small_first[:FIELDS - GATHER_FIELDS]
GATHERED = [f for f in range(FIELDS) if f not in ONE_HOT]
FIRST_HOT = len(GATHERED) - len(GATHERED) % 2
AFTER_HOT = FIRST_HOT + len(ONE_HOT)
ORDER = GATHERED[:FIRST_HOT] + ONE_HOT + GATHERED[FIRST_HOT:]
KC = [ROWS_OF[f] // TP for f in ONE_HOT]
KC_MAX = max(KC)
KC_KINDS = sorted(set(KC))
assert all(ROWS_OF[f] % TP == 0 for f in ONE_HOT)
PARTS = 3
PARTS_W = PARTS * DIM
RING = 4
AHEAD = 3
WARM_PRODUCTS = 16
LOTS = [range(0, 1), range(1, 2), range(2, 4), range(4, 7), range(7, 10), range(10, 13), range(13, 15),
        range(15, 17)]
LOT_MAX = max(map(len, LOTS))
FIRST_TILE = [0] * 8 + [1] * 9
IN_TILE_0 = FIRST_TILE.count(0)
EMB_ROWS = TILES * len(GATHERED) + len(ONE_HOT) - IN_TILE_0
assert LOTS[-1][-1] + 1 == len(ONE_HOT) == len(FIRST_TILE)
assert FIRST_HOT % 2 == IN_TILE_0 % 2 == AFTER_HOT % 2 == 0 or AFTER_HOT == FIELDS

CHUNKS = 7
BLOCKS = []
_at, _g = 0, FIELDS - 1
while _g > 0:
    _n = min(CHUNKS, _g)
    BLOCKS.append((_at, _g, _g - _n + 1, _n))
    _at, _g = _at + _g, _g - _n
DENSE_ROWS = 8
DENSE_AT = 128 - DENSE_ROWS
DENSE_CHUNK = BLOCKS[-1][3]
PAD_AT = 96
REPACKS = 2 * len(BLOCKS)
SP_BLOCKS, POOL_BLOCKS = BLOCKS[:2], BLOCKS[2:]
assert BLOCKS[-1][0] >= DENSE_AT and BLOCKS[-1][0] + BLOCKS[-1][1] <= 128


def zt_rows():
    rows = [[-1] * CHUNKS for _ in range(128)]
    for at, _, g0, n in BLOCKS:
        for c in range(n):
            for f in range(g0 + c):
                a, b = sorted((ORDER[f], ORDER[g0 + c]))
                rows[at + f][c] = a * FIELDS - a * (a + 1) // 2 + (b - a - 1)
    z = FIELDS * (FIELDS - 1) // 2
    for c in range(DENSE // DENSE_ROWS):
        for r in range(DENSE_ROWS):
            rows[DENSE_AT + r][DENSE_CHUNK + c] = z + c * DENSE_ROWS + r
    return rows


HOTS = len(ONE_HOT)


def hots(first, last):
    return [("hot", s) for s in range(first, last + 1)]


def turns(t, *groups):
    return [("turn", t, k) for k in groups]


def grams(t, first=0, end=GRAM_BATCHES):
    return [("gram", t, first, end)]


STEPS = (hots(0, 2) + turns(0, 0) + hots(3, 5) + turns(0, 1) + hots(6, 7) + turns(0, 2) + hots(8, 9) + turns(0, 3)
         + hots(10, 10) + turns(0, 4) + hots(11, 11) + grams(0, 0, 4) + turns(1, 3) + grams(0, 4, 8)
         + turns(1, 0) + hots(12, 12) + grams(0, 8) + turns(1, 1) + hots(13, 16)
         + turns(1, 2) + turns(2, 3) + turns(1, 4) + turns(2, 4) + grams(1, 0, 8)
         + turns(2, 0) + grams(1, 8) + [("l1", 0, 0)] + turns(2, 1) + [("l1", 0, 1), ("l2", 0)] + turns(2, 2)
         + turns(3, 3) + grams(2, 0, 4) + [("l3", 0)] + turns(3, 4) + grams(2, 4, 8) + turns(3, 0) + grams(2, 8)
         + [("l1", 1, 0), ("l1", 1, 1)] + turns(3, 1) + [("l2", 1)] + turns(3, 2) + [("l3", 1)]
         + grams(3) + [("l1", 2, 0), ("l1", 2, 1), ("l2", 2), ("l1", 3, 0), ("l3", 2), ("l1", 3, 1), ("l2", 3), ("l3", 3)])

ZEROS_AFTER, W2_AFTER = ([3, 4, 5, 6], [8, 9, 10, 12]), 12
ZERO_PIECE = TILE * FIELDS // len(ZEROS_AFTER[0])
TURNS = [step[1:] for step in STEPS if step[0] == "turn"]
assert sorted(TURNS) == [(t, k) for t in range(TILES) for k in range(GROUPS)]
assert [s[1] for s in STEPS if s[0] == "hot"] == list(range(HOTS))


def group_slots(k):
    return range(GROUP * k, min(GROUP * k + GROUP, FIELDS))


def is_hot(t, slot):
    return FIRST_HOT <= slot < AFTER_HOT and t >= FIRST_TILE[slot - FIRST_HOT]


def emb_row(t, slot):
    if FIRST_HOT <= slot < AFTER_HOT:
        return TILES * len(GATHERED) + slot - FIRST_HOT - IN_TILE_0
    return t * len(GATHERED) + (slot if slot < FIRST_HOT else slot - len(ONE_HOT))


def gather_order(t):
    return [*range(GROUPS)] if t == 0 else [GROUPS - 1, *range(GROUPS - 1)]


def gathered_slots(t, k):
    return [f for f in group_slots(k) if not is_hot(t, f)]


def evens_on_dve(t, k):
    return STEPS.index(("turn", t, k)) > STEPS.index(("hot", HOTS - 1))


def even_count(on_dve, n):
    return sum(evens_on_dve(*turn) == on_dve for turn in TURNS[:n + 1])


def last_turn(t):
    return max(n for n, turn in enumerate(TURNS) if turn[0] == t)


def takes_gram(n):
    return 1 if n < GRAM_BATCHES else n % 2


def gram_count(e, n):
    return sum(takes_gram(m) == e for m in range(n))


def batch_pairs(q):
    return range(PER_BANK * q, min(PER_BANK * q + PER_BANK, PAIRS))


def dlrm_kernel(nc, tables, ids, ids_hot, denseT, w1, b1, w2, b2, w3, eye, zeros, out):
    f32, i32 = mybir.dt.float32, mybir.dt.int32
    bf16, f16 = mybir.dt.bfloat16, mybir.dt.float16
    ACT = mybir.ActivationFunctionType
    ALU = mybir.AluOpType

    with ExitStack() as ctx:
        def sb(name, shape, dt=f32):
            return ctx.enter_context(nc.sbuf_tensor(name, shape, dt))

        def pb(name):
            return ctx.enter_context(nc.psum_tensor(name, [128, 512], f32))

        def sem(name):
            return ctx.enter_context(nc.semaphore(name))

        idx = sb("idx", [128, TILES * FIELDS], i32)
        ident = sb("ident", [128, 128])
        emb = sb("emb", [128, EMB_ROWS * DIM])
        looked_up = sb("looked_up", [128, TILES, PARTS, len(ONE_HOT) * DIM], bf16)
        embT = sb("embT", [128, 2, TILE * FIELDS])
        shared = sb("shared", [128, RING * KC_MAX * PARTS_W])
        grams = [sb("even_grams", [GW, GW, PAIRS])[:, :, :],
                 shared[0:GW, 0:GW * PAIRS].rearrange("p (n j) -> p n j", n=GW)]
        zT = sb("zT", [128, 2, CHUNKS, TILE])
        w2_sb = sb("w2_sb", [128, M1, H2])
        w3_sb = sb("w3_sb", [128, M2])
        b1_sb = sb("b1_sb", [128, M1])
        b2_sb = sb("b2_sb", [128, M2])
        h1 = sb("h1", [128, M1, TILE])
        h2 = sb("h2", [128, M2, TILE])
        y = sb("y", [1, BATCH])
        ids_all = sb("ids_all", [TP, 2, LOT_MAX, BATCH], i32)
        first_row = sb("first_row", [TP, len(KC_KINDS), 2])
        chunk_of = sb("chunk_of", [TP, AHEAD, 2, BATCH], f16)
        hot_words = sb("hot_words", [128, AHEAD * KC_MAX * BATCH // 2])
        hot = hot_words[0:TP, :].bitcast(bf16).rearrange("p (i k b) -> p i k b", i=AHEAD, k=KC_MAX)
        w1_sb = hot_words[:, 0:CHUNKS * H1].rearrange("p (c n) -> p c n", c=CHUNKS)
        ident_bf16 = ident[:, :].bitcast(bf16).rearrange("p (n two) -> p n two", two=2)[:, :, 1]
        parts_words = shared[0:TP, :]
        parts = parts_words.rearrange("p (i a k d) -> p i a k d", i=RING, k=KC_MAX, a=PARTS)
        halves = parts_words.bitcast(bf16)
        upper = halves.rearrange("p (i a k d two) -> p i a k d two", i=RING, k=KC_MAX, a=PARTS, two=2)

        turn_ps = [pb(f"turn_ps{i}") for i in range(2)]
        gram_ps = [pb(f"gram_ps{i}") for i in range(GRAM_BANKS)]
        wide_ps = [pb(f"wide_ps{i}") for i in range(2)]
        head_ps = pb("head_ps")
        y_ps = head_ps[0:1, TILE:2 * TILE]

        def l1_ps(m):
            return wide_ps[m % 2][:, 0:TILE]

        def l2_ps(m):
            return (head_ps, wide_ps[1])[m][:, 0:TILE]

        ids_in = sem("ids_in")
        ids_lot_in = [sem(f"ids_lot_in{i}") for i in range(len(LOTS))]
        ident_in = sem("ident_in")
        w1_in = sem("w1_in")
        small_in = sem("small_in")
        table_in = [sem(f"table_in{i}") for i in range(RING)]
        warm_zeros = sem("warm_zeros")
        zt_cleared = sem("zt_cleared")
        first_row_made = sem("first_row_made")
        chunk_of_made = sem("chunk_of_made")
        second_made = sem("second_made")
        zeros_in = [sem(f"zeros_in{i}") for i in range(2)]
        parts_made = sem("parts_made")
        hot_made = sem("hot_made")
        hot_done = sem("hot_done")
        hot_out = sem("hot_out")
        dense_in = [sem(f"dense_in{i}") for i in range(2)]
        gathered = [[sem(f"gathered{t}_{k}") for k in range(GROUPS)] for t in range(TILES)]
        turned = sem("turned")
        even_out = {True: sem("even_out_dve"), False: sem("even_out_act")}
        odd_out = sem("odd_out")
        gram_done = sem("gram_done")
        gram_out = [sem("gram_out_dve"), sem("gram_out_act")]
        repacked = [sem(f"repacked{i}") for i in range(2)]
        repacked_by_pool = sem("repacked_by_pool")
        l1_done = sem("l1_done")
        h1_out = sem("h1_out")
        l2_done = sem("l2_done")
        h2_out = sem("h2_out")
        l3_done = sem("l3_done")
        y_out = sem("y_out")
        stored = sem("stored")

        block = ctx.enter_context(nc.Block())

        def repack(eng, t, s, blocks, done):
            if t >= 2:
                eng.wait_ge(l1_done, M1 * (t - 1))
            for e in range(2):
                eng.wait_ge(gram_out[e], gram_count(e, GRAM_BATCHES * (t + 1)))
            for at, rows, g0, n in blocks:
                src = grams[t % 2][FIELDS * s:FIELDS * s + rows, FIELDS * s + g0:FIELDS * s + g0 + n, :]
                eng.dma_start(zT[at:at + rows, t % 2, 0:n, PAIRS * s:PAIRS * (s + 1)], src).then_inc(done, 16)

        def load_ids_lot(eng, n):
            lot = slice(LOTS[n][0], LOTS[n][-1] + 1)
            count = len(LOTS[n])
            if n >= 2:
                eng.wait_ge(chunk_of_made, 2 * LOTS[n - 1][0])
            src = ids_hot[lot, :].rearrange("(o s) b -> o (s b)", o=1).to_broadcast([TP, count * BATCH])
            eng.dma_start(ids_all[:, n % 2, 0:count, :].rearrange("p s b -> p (s b)"), src).then_inc(ids_lot_in[n], 16)

        @block.sync
        def _(sp):
            def load_table(s):
                if s >= RING:
                    sp.wait_ge(hot_done, 2 * (s - RING + 1))
                sp.dma_start(parts[:, s % RING, 0, 0:KC[s], :],
                             tables[ONE_HOT[s]].rearrange("(p k) d -> p k d", k=KC[s])).then_inc(table_in[s % RING], 16)

            sp.dma_start(idx[:, :], ids).then_inc(ids_in, 16)
            load_table(0)
            load_ids_lot(sp, 1)
            load_table(1)
            sp.dma_start(ident[:, :], eye).then_inc(ident_in, 16)
            load_ids_lot(sp, 2)
            load_table(2)
            load_ids_lot(sp, 3)
            for s in range(3, HOTS):
                for n in range(4, len(LOTS)):
                    if s == LOTS[n][0] - 2:
                        load_ids_lot(sp, n)
                load_table(s)
                for i in range(2):
                    if s in ZEROS_AFTER[i]:
                        at = ZERO_PIECE * ZEROS_AFTER[i].index(s)
                        sp.dma_start(embT[DIM:128, i, at:at + ZERO_PIECE],
                                     zeros.rearrange("(o n) -> o n", o=1).to_broadcast([128 - DIM, ZERO_PIECE]))\
                          .then_inc(zeros_in[i], 16)
                if s == W2_AFTER:
                    sp.dma_start(w2_sb[:, :, :], w2.rearrange("(k p) n -> p k n", p=128)).then_inc(small_in, 16)
                    with nc.allow_non_contiguous_dma(reason="a few hundred words"):
                        sp.dma_start(w3_sb[:, :], w3.rearrange("(k p) o -> p (k o)", p=128)).then_inc(small_in, 16)
                        sp.dma_start(b1_sb[:, :], b1.rearrange("(k p) -> p k", p=128)).then_inc(small_in, 16)
                        sp.dma_start(b2_sb[:, :], b2.rearrange("(k p) -> p k", p=128)).then_inc(small_in, 16)
            sp.wait_ge(zt_cleared, 1)
            for t in range(TILES):
                i = t % 2
                if t >= 2:
                    sp.wait_ge(l1_done, M1 * (t - 1))
                for c in range(DENSE // DENSE_ROWS):
                    sp.dma_start(zT[DENSE_AT:128, i, DENSE_CHUNK + c, :],
                                 denseT[DENSE_ROWS * c:DENSE_ROWS * (c + 1), TILE * t:TILE * (t + 1)])\
                      .then_inc(dense_in[i], 16)
                repack(sp, t, 0, BLOCKS, repacked[i])
                if t == 0:
                    sp.wait_ge(hot_done, 2 * HOTS)
                    sp.dma_start(w1_sb, w1.rearrange("p (c n) -> p c n", c=CHUNKS)).then_inc(w1_in, 16)
                repack(sp, t, 1, BLOCKS if t < TILES - 1 else SP_BLOCKS, repacked[i])
            sp.wait_ge(y_out, TILES)
            sp.dma_start(out.rearrange("b o -> o b"), y[:, :]).then_inc(stored, 16)
            sp.wait_ge(stored, 16)

        @block.gpsimd
        def _(pool):
            for i, kc in enumerate(KC_KINDS):
                ins = pool.iota(first_row[:, i, :], [[-(kc // 2), 2]], base=0, channel_multiplier=-kc,
                                allow_small_or_imprecise_dtypes=True)
            ins.then_inc(first_row_made, 1)
            pool.wait_ge(ids_in, 16)
            for t in range(TILES):
                for k in gather_order(t):
                    for f in gathered_slots(t, k):
                        at = t * FIELDS + f
                        pool.indirect_dma_start(
                            out=emb[:, DIM * emb_row(t, f):DIM * (emb_row(t, f) + 1)], out_offset=None, in_=tables[ORDER[f]],
                            in_offset=bass.IndirectOffsetOnAxis(ap=idx[:, at:at + 1], axis=0),
                        ).then_inc(gathered[t][k], 16)

            pool.wait_ge(zt_cleared, 1)
            repack(pool, TILES - 1, 1, POOL_BLOCKS, repacked_by_pool)

        def take_turned(copy, eng, t, k, odd, done):
            n = TURNS.index((t, k))
            slots = [f for f in group_slots(k) if f % 2 == odd]
            if t >= 2:
                eng.wait_ge(gram_done, GRAM_BATCHES * (t - 1))
            eng.wait_ge(turned, n + 1)
            src = turn_ps[n % 2][DIM * odd:DIM * odd + DIM, 0:TILE * len(slots)]
            dst = embT[0:DIM, t % 2, :].rearrange("d (b f) -> d f b", f=FIELDS)[:, slots[0]:slots[-1] + 1:2, :]
            copy(dst, src.rearrange("d (f b) -> d f b", b=TILE)).then_inc(done, 1)

        def take_grams(copy, eng, t, first, end, e):
            if t >= 2:
                eng.wait_ge(repacked[t % 2], 16 * REPACKS * (t // 2))
            for q in range(first, end):
                n = GRAM_BATCHES * t + q
                if takes_gram(n) != e:
                    continue
                pr = batch_pairs(q)
                eng.wait_ge(gram_done, n + 1)
                src = gram_ps[n % GRAM_BANKS][0:GW, 0:GW * len(pr)].rearrange("r (j n) -> r n j", n=GW)
                copy(grams[t % 2][:, :, pr[0]:pr[-1] + 1], src).then_inc(gram_out[e], 1)

        @block.vector
        def _(dve):
            def prepare_hot(s):
                i, kc = s % RING, KC[s]
                dve.wait_ge(table_in[i], 16 * (s // RING + 1))
                nc.vector.tensor_tensor(parts[:, i, 1, 0:kc, :], parts[:, i, 0, 0:kc, :], upper[:, i, 0, 0:kc, :, 1],
                                        ALU.subtract).then_inc(second_made, 1)
                dve.wait_ge(chunk_of_made, 2 * (s + 1))
                if s >= AHEAD:
                    dve.wait_ge(hot_done, 2 * (s - AHEAD + 1))
                first = TILE * FIRST_TILE[s]
                for k in range(kc // 2):
                    ins = nc.vector.tensor_scalar(hot[:, s % AHEAD, k:kc:kc // 2, first:], chunk_of[:, s % AHEAD, :, first:],
                                                  float(k), None, ALU.is_equal)
                ins.then_inc(hot_made, 1)
                dve.wait_ge(second_made, s + 1)
                nc.vector.tensor_tensor(parts[:, i, 2, 0:kc, :], parts[:, i, 1, 0:kc, :], upper[:, i, 1, 0:kc, :, 1],
                                        ALU.subtract).then_inc(parts_made, 1)

            nc.vector.memset(h1[:, :, :], 0.0).then_inc(warm_zeros, 1)
            nc.vector.memset(zT[PAD_AT:128, :, :, :], 0.0).then_inc(zt_cleared, 1)
            for step in STEPS:
                if step[0] == "hot":
                    prepare_hot(step[1])
                elif step[0] == "turn" and evens_on_dve(*step[1:]):
                    take_turned(nc.vector.tensor_copy, dve, step[1], step[2], 0, even_out[True])
                elif step[0] == "gram":
                    take_grams(nc.vector.tensor_copy, dve, *step[1:], 0)

        @block.scalar
        def _(act):
            def copy(dst, src):
                return nc.scalar.activation(dst, src, ACT.Copy)

            def take_looked_up(s, half):
                act.wait_ge(hot_done, 2 * s + half + 1)
                first = max(2 * half, FIRST_TILE[s])
                src = wide_ps[half][:, PARTS_W * (first % 2):2 * PARTS_W].rearrange("b (t a d) -> b t a d", a=PARTS, d=DIM)
                copy(looked_up[:, first:2 * half + 2, :, DIM * s:DIM * (s + 1)], src).then_inc(hot_out, 1)

            def place_ids(s, half):
                kind = KC_KINDS.index(KC[s])
                n = next(n for n, lot in enumerate(LOTS) if s in lot)
                if s == LOTS[n][0]:
                    act.wait_ge(ids_lot_in[n], 16)
                if s >= AHEAD:
                    act.wait_ge(hot_made, s - AHEAD + 1)
                nc.scalar.activation(chunk_of[:, s % AHEAD, half, :], ids_all[:, n % 2, s - LOTS[n][0], :],
                                     ACT.Identity, bias=first_row[:, kind, half:half + 1]).then_inc(chunk_of_made, 1)

            def take_l1(t, half):
                if t == 0:
                    act.wait_ge(small_in, 16 * 4)
                else:
                    act.wait_ge(l2_done, M2 * t)
                for m in (2 * half, 2 * half + 1):
                    act.wait_ge(l1_done, M1 * t + m + 1)
                    nc.scalar.activation(h1[:, m, :], l1_ps(m), ACT.Relu, bias=b1_sb[:, m:m + 1]).then_inc(h1_out, 1)

            def take_l2(t):
                if t >= 1:
                    act.wait_ge(l3_done, t)
                for m in range(M2):
                    act.wait_ge(l2_done, M2 * t + m + 1)
                    nc.scalar.activation(h2[:, m, :], l2_ps(m), ACT.Relu, bias=b2_sb[:, m:m + 1]).then_inc(h2_out, 1)

            def take_l3(t):
                act.wait_ge(l3_done, t + 1)
                copy(y[:, TILE * t:TILE * (t + 1)], y_ps).then_inc(y_out, 1)

            load_ids_lot(act, 0)
            act.wait_ge(first_row_made, 1)
            nc.scalar.activation(y[:, 0:1], first_row[0:1, 0, 0:1], ACT.Identity)
            for s in range(AHEAD):
                for half in range(2):
                    place_ids(s, half)
            for step in STEPS:
                if step[0] == "hot":
                    for half in range(2):
                        take_looked_up(step[1], half)
                        if step[1] + AHEAD < HOTS:
                            place_ids(step[1] + AHEAD, half)
                elif step[0] == "turn":
                    t, k = step[1:]
                    if not evens_on_dve(t, k):
                        take_turned(copy, act, t, k, 0, even_out[False])
                    take_turned(copy, act, t, k, 1, odd_out)
                elif step[0] == "gram":
                    take_grams(copy, act, *step[1:], 1)
                elif step[0] == "l1":
                    take_l1(*step[1:])
                elif step[0] == "l2":
                    take_l2(step[1])
                else:
                    take_l3(step[1])

        @block.tensor
        def _(pe):
            def look_up(s):
                i, kc = s % RING, KC[s]
                pe.wait_ge(hot_made, s + 1)
                pe.wait_ge(parts_made, s + 1)
                for t in range(FIRST_TILE[s], TILES):
                    if s >= 1 and t in (FIRST_TILE[s], 2):
                        pe.wait_ge(hot_out, 2 * (s - 1) + t // 2 + 1)
                    for k in range(kc):
                        ins = nc.tensor.matmul(wide_ps[t // 2][:, PARTS_W * (t % 2):PARTS_W * (t % 2 + 1)],
                                               hot[:, s % AHEAD, k, TILE * t:TILE * (t + 1)], upper[:, i, :, k, :, 1],
                                               start=(k == 0), stop=(k == kc - 1))
                    if t % 2:
                        ins.then_inc(hot_done, 1)

            def turn(t, k):
                n = TURNS.index((t, k))
                if n == 0:
                    pe.wait_ge(ident_in, 16)
                slots = group_slots(k)
                if gathered_slots(t, k):
                    pe.wait_ge(gathered[t][k], 16 * len(gathered_slots(t, k)))
                hot_slots = [f for f in slots if is_hot(t, f)]
                if hot_slots:
                    pe.wait_ge(hot_out, 2 * (hot_slots[-1] - FIRST_HOT) + t // 2 + 1)
                if n >= 2:
                    on_dve = evens_on_dve(*TURNS[n - 2])
                    pe.wait_ge(even_out[on_dve], even_count(on_dve, n - 2))
                    pe.wait_ge(odd_out, n - 1)
                for j, f in enumerate(slots[::2]):
                    w = DIM * min(2, FIELDS - f)
                    dst = turn_ps[n % 2][0:w, TILE * j:TILE * (j + 1)]
                    if is_hot(t, f):
                        at = DIM * (f - FIRST_HOT)
                        for a in range(PARTS):
                            ins = nc.tensor.matmul(dst, looked_up[:, t, a, at:at + w], ident_bf16,
                                                   start=(a == 0), stop=(a == PARTS - 1))
                    else:
                        at = DIM * emb_row(t, f)
                        ins = nc.tensor.transpose(dst, emb[:, at:at + w], ident[:, :])
                ins.then_inc(turned, 1)

            def gram(t, first, end):
                n = last_turn(t)
                for on_dve in (False, True):
                    if even_count(on_dve, n):
                        pe.wait_ge(even_out[on_dve], even_count(on_dve, n))
                pe.wait_ge(odd_out, n + 1)
                if t < 2:
                    pe.wait_ge(zeros_in[t], 16 * len(ZEROS_AFTER[t]))
                for q in range(first, end):
                    n = GRAM_BATCHES * t + q
                    if n >= GRAM_BANKS:
                        e = takes_gram(n - GRAM_BANKS)
                        pe.wait_ge(gram_out[e], gram_count(e, n - GRAM_BANKS + 1))
                    for c, j in enumerate(batch_pairs(q)):
                        pair = embT[:, t % 2, GW * j:GW * (j + 1)]
                        ins = nc.tensor.matmul(gram_ps[n % GRAM_BANKS][0:GW, GW * c:GW * (c + 1)], pair, pair,
                                               start=True, stop=True)
                    ins.then_inc(gram_done, 1)

            def layer1(t, half):
                i = t % 2
                if t == 0:
                    pe.wait_ge(w1_in, 16)
                    pe.wait_ge(small_in, 16 * 4)
                    pe.wait_ge(hot_out, 2 * HOTS)
                pe.wait_ge(dense_in[i], 16 * (DENSE // DENSE_ROWS) * (t // 2 + 1))
                if t < TILES - 1:
                    pe.wait_ge(repacked[i], 16 * REPACKS * (t // 2 + 1))
                else:
                    pe.wait_ge(repacked[i], 16 * (REPACKS * (t // 2 + 1) - len(POOL_BLOCKS)))
                    pe.wait_ge(repacked_by_pool, 16 * len(POOL_BLOCKS))
                for m in (2 * half, 2 * half + 1):
                    if m >= 2:
                        pe.wait_ge(h1_out, M1 * t + m - 1)
                    elif t >= 1:
                        pe.wait_ge(h1_out, M1 * (t - 1) + m + 3)
                        if m == 1:
                            pe.wait_ge(h2_out, M2 * t)
                    for c in range(CHUNKS):
                        ins = nc.tensor.matmul(l1_ps(m), w1_sb[:, c, 128 * m:128 * (m + 1)], zT[:, i, c, :],
                                               start=(c == 0), stop=(c == CHUNKS - 1))
                    ins.then_inc(l1_done, 1)

            def layer2(t):
                if t >= 1:
                    pe.wait_ge(y_out, t)
                for m in range(M2):
                    for k in range(M1):
                        pe.wait_ge(h1_out, M1 * t + k + 1)
                        ins = nc.tensor.matmul(l2_ps(m), w2_sb[:, k, 128 * m:128 * (m + 1)], h1[:, k, :],
                                               start=(k == 0), stop=(k == M1 - 1))
                    ins.then_inc(l2_done, 1)

            def layer3(t):
                for k in range(M2):
                    pe.wait_ge(h2_out, M2 * t + k + 1)
                    ins = nc.tensor.matmul(y_ps, w3_sb[:, k:k + 1], h2[:, k, :],
                                           start=(k == 0), stop=(k == M2 - 1))
                ins.then_inc(l3_done, 1)

            pe.wait_ge(warm_zeros, 1)
            zero_words = h1[:, :, :].rearrange("p m b -> p (m b)").bitcast(bf16)
            for _ in range(WARM_PRODUCTS):
                nc.tensor.matmul(gram_ps[0][:, :], zero_words[:, 0:128], zero_words[:, 512:1024], start=True, stop=True)
            for step in STEPS:
                if step[0] == "hot":
                    look_up(step[1])
                elif step[0] == "turn":
                    turn(step[1], step[2])
                elif step[0] == "gram":
                    gram(*step[1:])
                elif step[0] == "l1":
                    layer1(*step[1:])
                elif step[0] == "l2":
                    layer2(step[1])
                else:
                    layer3(step[1])


def kernel(**inputs):
    import numpy as np
    import concourse.bacc as bacc
    from concourse.bass_utils import run_bass_kernel_spmd as run

    nc = bacc.Bacc("TRN2", target_bir_lowering=False, num_devices=1)
    arrays = {}

    def dram(name, a):
        a = np.ascontiguousarray(a)
        arrays[name] = a
        return nc.dram_tensor(name, a.shape, mybir.dt.from_np(a.dtype), kind="ExternalInput").ap()

    tables = [dram(f"tbl_{f}", np.asarray(inputs[f"tbl_{f}"])) for f in range(FIELDS)]
    ids = np.asarray(inputs["ids"]).reshape(TILES, 2, PAIRS, FIELDS).transpose(0, 2, 1, 3).reshape(BATCH, FIELDS)
    w1 = np.asarray(inputs["W_top1"])
    w1_rows = np.concatenate([w1, np.zeros((1, H1), w1.dtype)])[np.array(zt_rows())]
    args = dict(
        ids=dram("ids", ids[:, ORDER].reshape(TILES, TILE, FIELDS).transpose(1, 0, 2).reshape(TILE, -1)),
        ids_hot=dram("ids_hot", ids[:, ONE_HOT].T),
        denseT=dram("denseT", np.asarray(inputs["dense_ctx"]).T),
        w1=dram("w1", w1_rows.reshape(128, CHUNKS * H1)),
        b1=dram("b1", np.asarray(inputs["b_top1"])),
        w2=dram("w2", np.asarray(inputs["W_top2"])),
        b2=dram("b2", np.asarray(inputs["b_top2"])),
        w3=dram("w3", np.asarray(inputs["W_top3"])),
        eye=dram("eye", np.eye(128, dtype=np.float32)),
        zeros=dram("zeros", np.zeros(ZERO_PIECE, np.float32)),
    )
    out = nc.dram_tensor("out_y", (BATCH, 1), mybir.dt.float32, kind="ExternalOutput").ap()
    dlrm_kernel(nc, tables, out=out, **args)
    r = run(nc, [arrays], core_ids=[0])
    return r.results[0]["out_y"]
```
